# Optimizing a Trainium2 kernel written in Bass

```python
import numpy as np
import jax
import jax.numpy as jnp

def _softmax(x, axis=-1):
    return jax.nn.softmax(x, axis=axis)

def _gelu(x):
    return jax.nn.gelu(x, approximate=True)

def _silu(x):
    return jax.nn.silu(x)

def _sigmoid(x):
    return jax.nn.sigmoid(x)

def _layernorm(x, axis=-1, eps=1e-05):
    m = jnp.mean(x, axis=axis, keepdims=True)
    v = jnp.var(x, axis=axis, keepdims=True)
    return (x - m) / jnp.sqrt(v + eps)

def _scatter_add(tgt, idx, src, axis=0):
    return tgt.at[idx].add(src)

def _segment_sum(src, seg, n):
    return jax.ops.segment_sum(src, seg, n)
kernel_name = 'mk_gnn_preln_d1_gnn_r8_38d407'

def setup_inputs(seed: int=0):
    np.random.seed(seed)
    _w = jnp.asarray

    def _rec_inputs():
        import jax
        import jax.numpy as jnp
        _gk = jax.random.key(seed)
        x = -0.0001006 + 1 * jax.random.normal(jax.random.fold_in(_gk, 1), (6250, 96), jnp.float32)
        _s = jax.random.randint(jax.random.fold_in(_gk, 2), (50000,), 0, 6250, jnp.int32)
        _d = jax.random.randint(jax.random.fold_in(_gk, 3), (50000,), 0, 6250, jnp.int32)
        _loop = jnp.arange(6250, dtype=jnp.int32)
        src = jnp.concatenate([_s, _d, _loop])
        dst = jnp.concatenate([_d, _s, _loop])
        _o = jnp.argsort(dst, stable=True)
        src = src[_o]
        dst = dst[_o]
        edge_attr_96 = 5.93493e-05 + 1.00006 * jax.random.normal(jax.random.fold_in(_gk, 11), (106250, 96), jnp.float32)
        return (x, src, dst, edge_attr_96)
    x, src, dst, edge_attr_96 = _rec_inputs()

    def _L0_gnn_setup():
        import jax, jax.numpy as jnp
        import numpy as np
        N_NODES = 6250
        N_EDGES = 100000
        NIN = 96
        NOUT = 96
        key = jax.random.key(seed)
        ks = jax.random.split(key, 10)
        s = 1.0 / np.sqrt(NIN)
        so = 1.0 / np.sqrt(NOUT)
        return {'x': jax.random.normal(ks[0], (N_NODES, NIN), dtype=jnp.float32), 'edge_index': jax.random.randint(ks[1], (2, N_EDGES), 0, N_NODES, dtype=jnp.int64), 'edge_attr': jax.random.normal(ks[2], (N_EDGES, NIN), dtype=jnp.float32), 'W_edge': jax.random.uniform(ks[3], (NIN, NIN), jnp.float32, -s, s), 'b_edge': jax.random.uniform(ks[4], (NIN,), jnp.float32, -s, s), 'eps': jnp.zeros((), dtype=jnp.float32), 'W1': jax.random.uniform(ks[5], (NOUT, NIN), jnp.float32, -s, s), 'b1': jax.random.uniform(ks[6], (NOUT,), jnp.float32, -s, s), 'W2': jax.random.uniform(ks[7], (NOUT, NOUT), jnp.float32, -so, so), 'b2': jax.random.uniform(ks[8], (NOUT,), jnp.float32, -so, so)}
    _L0_gnn_all = _L0_gnn_setup()
    _L0_gnn_in = {k: v for k, v in _L0_gnn_all.items() if k in ('W_edge', 'b_edge', 'eps', 'W1', 'b1', 'W2', 'b2')}
    del _L0_gnn_all
    return {'x': x, 'src': src, 'dst': dst, 'edge_attr_96': edge_attr_96, 'L0_gnn_W_edge': _L0_gnn_in['W_edge'], 'L0_gnn_b_edge': _L0_gnn_in['b_edge'], 'L0_gnn_eps': _L0_gnn_in['eps'], 'L0_gnn_W1': _L0_gnn_in['W1'], 'L0_gnn_b1': _L0_gnn_in['b1'], 'L0_gnn_W2': _L0_gnn_in['W2'], 'L0_gnn_b2': _L0_gnn_in['b2']}

def reference(x, src, dst, edge_attr_96, L0_gnn_W_edge, L0_gnn_b_edge, L0_gnn_eps, L0_gnn_W1, L0_gnn_b1, L0_gnn_W2, L0_gnn_b2):
    import jax
    import jax.numpy as jnp

    def _L0_gnn_ref(x, edge_index, edge_attr, W_edge, b_edge, eps, W1, b1, W2, b2):
        import jax, jax.numpy as jnp
        import numpy as np
        N_NODES = 6250
        N_EDGES = 100000
        NIN = 96
        NOUT = 96
        ea = edge_attr @ W_edge.T + b_edge
        src, dst = (edge_index[0], edge_index[1])
        msg = jax.nn.relu(x[src] + ea)
        aggr = jax.ops.segment_sum(msg, dst, num_segments=N_NODES)
        h = (1.0 + eps) * x + aggr
        h = jax.nn.relu(h @ W1.T + b1)
        return h @ W2.T + b2
    edge_index = jnp.stack([src, dst])
    h = jnp.maximum(_layernorm(x, axis=-1), 0.0)
    x = x + _L0_gnn_ref(h, edge_index, edge_attr_96, L0_gnn_W_edge, L0_gnn_b_edge, L0_gnn_eps, L0_gnn_W1, L0_gnn_b1, L0_gnn_W2, L0_gnn_b2)
    return x

_drawn_inputs = setup_inputs


def setup_inputs(seed=0):
    import zlib

    import numpy as np

    out = dict(_drawn_inputs(seed))
    spreads = {}
    factors = {'L0_gnn_b1': 6.168}
    for name, (base, spread) in spreads.items():
        noise = np.random.default_rng([zlib.crc32(name.encode()), seed]).standard_normal(out[name].shape)
        drawn = base * np.exp(spread * noise) if base else spread * noise
        out[name] = jnp.asarray(drawn.astype(out[name].dtype))
    for name, factor in factors.items():
        out[name] = (out[name] * factor).astype(out[name].dtype)
    return out
```

```python
from contextlib import ExitStack

import numpy as np

import concourse.bass as bass
from concourse import mybir

ALU = mybir.AluOpType
ACT = mybir.ActivationFunctionType
F32 = mybir.dt.float32
I32 = mybir.dt.int32
AX = mybir.AxisListType

EDGE_TILE = 128
GROUP_TILES = 10
HALF_TILES = 5
WINDOW = 128
BANK = 512
LN_EPS = 1e-5


def node_layout(nodes):
    per = next(n for n in range(1, nodes + 1) if nodes % n == 0 and nodes // n <= 128)
    return nodes // per, per


def engine_spread(parts):
    whole = parts - parts % 16
    return [(0, whole)] + ([(whole, parts)] if whole < parts else [])


def gnn_layer(nc, x, edge_blocks, edge_tail, meta_blocks, src_tail, dst_tail, dst_rows, w_edge_t, b_edge,
              eps, w1_t, b1, w2_t, b2, out):
    N, D = x.shape
    GROUPS, _, GE = edge_blocks.shape
    TAIL = edge_tail.shape[1]
    NP, PER = node_layout(N)
    PAIRS = GROUPS // 2
    assert GROUPS % 2 == 1 and GE == GROUP_TILES * EDGE_TILE and 0 < TAIL <= EDGE_TILE
    assert HALF_TILES * D <= BANK and D % 32 == 0 and D < 128
    HALF = HALF_TILES * D
    JT = BANK // NP
    node_chunks = [(j, min(j + JT, PER)) for j in range(0, PER, JT)]
    NCH = len(node_chunks)
    ROWS = GROUPS + 1
    spread = engine_spread(NP)

    h_table = nc.dram_tensor("h_table", (N, D), F32, kind="Internal").ap()

    with ExitStack() as ctx:
        def sb(name, shape, dt=F32):
            return ctx.enter_context(nc.sbuf_tensor(name, shape, dt))

        def psum(name, shape, dt=F32):
            return ctx.enter_context(nc.psum_tensor(name, shape, dt))

        def sem(name):
            return ctx.enter_context(nc.semaphore(name))

        x_all = sb("x_all", [NP, PER * D])
        h_all = sb("h_all", [NP, PER * D])
        stats = sb("stats", [NP, PER, 6])
        moments = sb("moments", [NP, PER, 2])
        std = sb("std", [NP, PER])
        rstd = sb("rstd", [NP, PER])
        eps_col = sb("eps_col", [128, 1])
        acc = sb("acc", [D, N + WINDOW])
        scale_eps = sb("scale_eps", [D, 1])
        scale_one_eps = sb("scale_one_eps", [D, 1])
        w_edge = sb("w_edge", [D + 1, D])
        w1 = sb("w1", [D, D])
        b1_col = sb("b1_col", [D, 1])
        w2 = sb("w2", [D + 1, D])
        ident = sb("ident", [128, 128])
        iota_sb = sb("iota_sb", [128, WINDOW])
        dst_by_row = sb("dst_by_row", [ROWS, GE], I32)
        first_last = sb("first_last", [ROWS, 2])
        bounds_f = sb("bounds_f", [128, 2 * ROWS])
        bounds_i = sb("bounds_i", [1, 2 * ROWS], I32)
        edge_in = [sb(f"edge_in{b}", [D + 1, GE]) for b in range(2)]
        meta = [sb(f"meta{b}", [128, 2 * GROUP_TILES], I32) for b in range(2)]
        gathered = [sb(f"gathered{b}", [128, GROUP_TILES * D]) for b in range(2)]
        msg = [sb(f"msg{b}", [128, GROUP_TILES * D]) for b in range(2)]
        dst_rel = sb("dst_rel", [128, GROUP_TILES])
        select = sb("select", [128, GROUP_TILES, WINDOW])
        edge_tail_in = sb("edge_tail_in", [D + 1, TAIL])
        src_tail_in = sb("src_tail_in", [TAIL, 1], I32)
        dst_tail_in = sb("dst_tail_in", [TAIL, 1], I32)
        hidden = [sb(f"hidden{b}", [D + 1, JT * NP]) for b in range(2)]

        edge_ps = [[psum(f"edge_ps{b}{i}", [128, BANK]) for i in range(2)] for b in range(2)]
        agg_ps = psum("agg_ps", [128, BANK])
        iota_ps = psum("iota_ps", [128, BANK])
        work_ps = [psum(f"work_ps{b}", [128, BANK]) for b in range(2)]

        x_in = sem("x_in")
        dst_in = sem("dst_in")
        weights_in = sem("weights_in")
        ident_made = sem("ident_made")
        iota_made = sem("iota_made")
        iota_copied = sem("iota_copied")
        ones_set = sem("ones_set")
        stats_done = sem("stats_done")
        std_done = sem("std_done")
        normed = sem("normed")
        dve_step = sem("dve_step")
        h_done = sem("h_done")
        table_stored = sem("table_stored")
        bounds_min_max = sem("bounds_min_max")
        bounds_spread = sem("bounds_spread")
        bounds_ready = sem("bounds_ready")
        h_turned = sem("h_turned")
        acc_ready = sem("acc_ready")
        edges_in = [sem(f"edges_in{b}") for b in range(2)]
        meta_in = [sem(f"meta_in{b}") for b in range(2)]
        gather_in = [[sem(f"gather_in{b}{i}") for i in range(2)] for b in range(2)]
        tail_in = sem("tail_in")
        tail_gather_in = sem("tail_gather_in")
        edge_done = sem("edge_done")
        added = sem("added")
        relu_done = sem("relu_done")
        select_made = sem("select_made")
        agg_done = sem("agg_done")
        mlp1_done = sem("mlp1_done")
        mlp_relu_done = sem("mlp_relu_done")
        mlp2_done = sem("mlp2_done")
        result_done = sem("result_done")
        stored = sem("stored")
        acc_final = sem("acc_final")
        gather_cleared = sem("gather_cleared")
        one_eps_set = sem("one_eps_set")
        offsets_made = sem("offsets_made")
        acc_summed = sem("acc_summed")

        x_dram = x.rearrange("(p j) d -> p (j d)", p=NP)
        table_dram = h_table.rearrange("(p j) d -> p (j d)", p=NP)
        out_dram = out.rearrange("(p j) d -> p (j d)", p=NP)
        acc_nodes = acc[:, 0:N].rearrange("f (p j) -> f j p", p=NP)

        N_WEIGHTS = 7

        block = ctx.enter_context(nc.Block())

        @block.sync
        def _(sp):
            for a, b in spread:
                sp.dma_start(x_all[a:b, :], x_dram[a:b, :]).then_inc(x_in, 16)
            sp.dma_start(dst_by_row[:], dst_rows).then_inc(dst_in, 16)
            sp.dma_start(w_edge[0:D, :], w_edge_t).then_inc(weights_in, 16)
            sp.dma_start(w_edge[D:D + 1, :], b_edge.rearrange("(a d) -> a d", a=1)).then_inc(weights_in, 16)
            sp.dma_start(w1[:], w1_t).then_inc(weights_in, 16)
            sp.dma_start(b1_col[:], b1.rearrange("(d a) -> d a", a=1)).then_inc(weights_in, 16)
            sp.dma_start(w2[0:D, :], w2_t).then_inc(weights_in, 16)
            sp.dma_start(w2[D:D + 1, :], b2.rearrange("(a d) -> a d", a=1)).then_inc(weights_in, 16)
            sp.dma_start(scale_eps[:], eps.rearrange("(a b) -> a b", a=1).broadcast_to((D, 1))).then_inc(weights_in, 16)
            sp.dma_start(edge_tail_in[0:D, :], edge_tail).then_inc(tail_in, 16)
            sp.dma_start(src_tail_in[:], src_tail.rearrange("(e a) -> e a", a=1)).then_inc(tail_in, 16)
            sp.dma_start(dst_tail_in[:], dst_tail.rearrange("(e a) -> e a", a=1)).then_inc(tail_in, 16)

            def load(b, g):
                sp.dma_start(meta[b][:], meta_blocks[g]).then_inc(meta_in[b], 16)
                sp.dma_start(edge_in[b][0:D, :], edge_blocks[g]).then_inc(edges_in[b], 16)

            load(0, 0)
            load(1, 1)
            sp.wait_ge(h_done, 1)
            for a, b in spread:
                sp.dma_start(table_dram[a:b, :], h_all[a:b, :]).then_inc(table_stored, 16)
            with sp.Fori(1, PAIRS) as p:
                for b in range(2):
                    sp.wait_ge(added, 4 * p - 2 + 2 * b)
                    sp.wait_ge(edge_done, 2 * p - 1 + b)
                    load_at = meta_blocks[bass.ds(2 * p + b, 1)].rearrange("a e t -> (a e) t")
                    sp.dma_start(meta[b][:], load_at).then_inc(meta_in[b], 16)
                    edges_at = edge_blocks[bass.ds(2 * p + b, 1)].rearrange("a d e -> (a d) e")
                    sp.dma_start(edge_in[b][0:D, :], edges_at).then_inc(edges_in[b], 16)
            sp.wait_ge(added, 2 * (GROUPS - 2))
            sp.wait_ge(edge_done, GROUPS - 2)
            load(0, GROUPS - 1)
            for c, (j0, j1) in enumerate(node_chunks):
                sp.wait_ge(result_done, c + 1)
                for a, b in spread:
                    sp.dma_start(out_dram[a:b, j0 * D:j1 * D], x_all[a:b, j0 * D:j1 * D]).then_inc(stored, 16)
            sp.wait_ge(stored, 16 * NCH * len(spread))

        @block.gpsimd
        def _(pool):
            nc.gpsimd.memset(ident[:], 0.0).then_inc(ident_made, 1)
            pool.wait_ge(ident_made, 1)
            nc.gpsimd.affine_select(out=ident[:], in_=ident[:], compare_op=ALU.not_equal, fill=1.0, base=0,
                                    pattern=[[-1, 128]], channel_multiplier=1).then_inc(ident_made, 1)
            nc.gpsimd.iota(iota_sb[:], [[1, WINDOW]], base=0, channel_multiplier=0,
                           allow_small_or_imprecise_dtypes=True).then_inc(iota_made, 1)

            def gather(b, t):
                half = t // HALF_TILES
                nc.gpsimd.indirect_dma_start(
                    out=gathered[b][:, t * D:(t + 1) * D], out_offset=None, in_=h_table,
                    in_offset=bass.IndirectOffsetOnAxis(ap=meta[b][:, t:t + 1], axis=0),
                ).then_inc(gather_in[b][half], 16)

            def gather_group(b):
                for t in range(GROUP_TILES):
                    gather(b, t)

            pool.wait_ge(table_stored, 16 * len(spread))
            for b in range(2):
                pool.wait_ge(meta_in[b], 16)
                gather_group(b)
            with pool.Fori(1, PAIRS) as p:
                for b in range(2):
                    pool.wait_ge(meta_in[b], 16 * p + 16).then_inc(gather_cleared, 1)
                    pool.wait_ge(added, 4 * p - 2 + 2 * b).then_inc(gather_cleared, 1)
                    gather_group(b)
            pool.wait_ge(meta_in[0], 16 * PAIRS + 16)
            pool.wait_ge(added, 4 * PAIRS - 2)
            gather_group(0)
            pool.wait_ge(tail_in, 48)
            pool.wait_ge(added, 4 * PAIRS)
            nc.gpsimd.indirect_dma_start(
                out=gathered[1][0:TAIL, 0:D], out_offset=None, in_=h_table,
                in_offset=bass.IndirectOffsetOnAxis(ap=src_tail_in[:, 0:1], axis=0),
            ).then_inc(tail_gather_in, 16)

        @block.scalar
        def _(act):
            act.wait_ge(iota_made, 1)
            nc.scalar.copy(iota_ps[:, 0:WINDOW], iota_sb[:]).then_inc(iota_copied, 1)
            act.wait_ge(stats_done, 1)
            nc.scalar.activation(std[:], moments[:, :, 1], ACT.Sqrt, bias=eps_col[0:NP, :]).then_inc(std_done, 1)
            act.wait_ge(normed, 1)
            nc.scalar.activation(h_all[:], h_all[:], ACT.Relu).then_inc(h_done, 1)
            act.wait_ge(one_eps_set, 1)
            for c, (j0, j1) in enumerate(node_chunks):
                act.wait_ge(h_turned, c + 1)
                nc.scalar.activation(acc_nodes[:, j0:j1, :],
                                     work_ps[c % 2][0:D, 0:(j1 - j0) * NP].rearrange("f (j p) -> f j p", p=NP),
                                     ACT.Copy, scale=scale_one_eps[:, 0:1]).then_inc(acc_ready, 1)

            def relu_half(b, i, count):
                act.wait_ge(added, count)
                nc.scalar.activation(msg[b][:, i * HALF:(i + 1) * HALF], msg[b][:, i * HALF:(i + 1) * HALF],
                                     ACT.Relu).then_inc(relu_done, 1)

            with act.Fori(0, PAIRS) as p:
                for b in range(2):
                    for i in range(2):
                        relu_half(b, i, 4 * p + 2 * b + i + 1)
            for i in range(2):
                relu_half(0, i, 4 * PAIRS + i + 1)
            act.wait_ge(added, 4 * PAIRS + 3)
            nc.scalar.activation(msg[1][0:TAIL, 0:D], msg[1][0:TAIL, 0:D], ACT.Relu).then_inc(relu_done, 1)

            for c, (j0, j1) in enumerate(node_chunks):
                act.wait_ge(mlp1_done, c + 1)
                if c >= 2:
                    act.wait_ge(mlp2_done, c - 1)
                n = (j1 - j0) * NP
                nc.scalar.activation(hidden[c % 2][0:D, 0:n], work_ps[c % 2][0:D, 0:n], ACT.Relu,
                                     bias=b1_col[:, 0:1]).then_inc(mlp_relu_done, 1)

        @block.tensor
        def _(pe):
            pe.wait_ge(ident_made, 2)
            pe.wait_ge(bounds_min_max, 2)
            for k in range(2):
                mm = pe.matmul(agg_ps[:, k * ROWS:(k + 1) * ROWS], first_last[:, k:k + 1].broadcast_to((ROWS, 128)),
                               ident[0:ROWS, 0:ROWS], start=True, stop=True)
            mm.then_inc(bounds_spread, 1)
            pe.wait_ge(h_done, 1)
            for c, (j0, j1) in enumerate(node_chunks):
                if c >= 2:
                    pe.wait_ge(acc_ready, c - 1)
                for j in range(j0, j1):
                    mm = pe.transpose(work_ps[c % 2][0:D, (j - j0) * NP:(j - j0 + 1) * NP],
                                      h_all[:, j * D:(j + 1) * D], ident[0:NP, 0:NP])
                mm.then_inc(h_turned, 1)

            def edge_features(b):
                for t in range(GROUP_TILES):
                    at = (t % HALF_TILES) * D
                    mm = pe.matmul(edge_ps[b][t // HALF_TILES][:, at:at + D],
                                   edge_in[b][:, t * EDGE_TILE:(t + 1) * EDGE_TILE], w_edge[:],
                                   start=True, stop=True)
                mm.then_inc(edge_done, 1)

            window = pe.alloc_register("pe_window")
            pe.reg_mov(window, 1)

            def sum_windows(b, row, tiles, parts):
                first = pe.value_load(bounds_i[0:1, bass.ds(row, 1)], min_val=0, max_val=N - 1)
                last = pe.value_load(bounds_i[0:1, bass.ds(row + ROWS, 1)], min_val=0, max_val=N - 1)
                with pe.Fori(first, last + 1, WINDOW):
                    this_window = pe.snap(window)
                    pe.wait_ge(select_made, this_window)
                    for t in range(tiles):
                        mm = pe.matmul(agg_ps[0:D, 0:WINDOW], msg[b][0:parts, t * D:(t + 1) * D],
                                       select[0:parts, t, :], start=(t == 0), stop=(t == tiles - 1))
                    mm.then_inc(agg_done, 1)
                    pe.reg_add(window, window, 1)

            pe.wait_ge(weights_in, 16 * N_WEIGHTS)
            pe.wait_ge(ones_set, 1)
            pe.wait_ge(edges_in[0], 16)
            edge_features(0)
            pe.wait_ge(bounds_ready, 2)
            pe.wait_ge(edges_in[1], 16)
            edge_features(1)
            with pe.Fori(0, PAIRS - 1) as p:
                for b in range(2):
                    pe.wait_ge(relu_done, 4 * p + 2 * b + 2)
                    sum_windows(b, 2 * p + b, GROUP_TILES, 128)
                    pe.wait_ge(edges_in[b], 16 * p + 32)
                    edge_features(b)
            pe.wait_ge(relu_done, 4 * PAIRS - 2)
            sum_windows(0, GROUPS - 3, GROUP_TILES, 128)
            pe.wait_ge(edges_in[0], 16 * PAIRS + 16)
            edge_features(0)
            pe.wait_ge(relu_done, 4 * PAIRS)
            sum_windows(1, GROUPS - 2, GROUP_TILES, 128)
            pe.wait_ge(tail_in, 48)
            pe.matmul(edge_ps[1][0][0:TAIL, 0:D], edge_tail_in[:], w_edge[:], start=True, stop=True).then_inc(edge_done, 1)
            pe.wait_ge(relu_done, 4 * PAIRS + 2)
            sum_windows(0, GROUPS - 1, GROUP_TILES, 128)
            pe.wait_ge(relu_done, 4 * PAIRS + 3)
            sum_windows(1, GROUPS, 1, TAIL)

            def first_layer(c):
                j0, j1 = node_chunks[c]
                n = (j1 - j0) * NP
                if c == 0:
                    pe.wait_ge(acc_final, 1)
                if c >= 2:
                    pe.wait_ge(mlp_relu_done, c - 1)
                pe.matmul(work_ps[c % 2][0:D, 0:n].rearrange("f (j p) -> f j p", p=NP), w1[:],
                          acc_nodes[:, j0:j1, :], start=True, stop=True).then_inc(mlp1_done, 1)

            first_layer(0)
            for c, (j0, j1) in enumerate(node_chunks):
                if c + 1 < NCH:
                    first_layer(c + 1)
                pe.wait_ge(mlp_relu_done, c + 1)
                if c >= 2:
                    pe.wait_ge(result_done, c - 1)
                for j in range(j1 - j0):
                    mm = pe.matmul(edge_ps[0][c % 2][0:NP, j * D:(j + 1) * D], hidden[c % 2][:, j * NP:(j + 1) * NP],
                                   w2[:], start=True, stop=True)
                mm.then_inc(mlp2_done, 1)

        @block.vector
        def _(dve):
            steps = [0]

            def ordered(instruction):
                steps[0] += 1
                instruction.then_inc(dve_step, 1)
                dve.wait_ge(dve_step, steps[0])

            nc.vector.memset(eps_col[:], LN_EPS)
            nc.vector.memset(dst_rel[:], 0.0).then_inc(offsets_made, 1)
            nc.vector.memset(acc[:, N:N + WINDOW], 0.0).then_inc(acc_summed, 1)
            nc.vector.memset(edge_in[0][D:D + 1, :], 1.0)
            nc.vector.memset(edge_in[1][D:D + 1, :], 1.0)
            nc.vector.memset(edge_tail_in[D:D + 1, :], 1.0)
            nc.vector.memset(hidden[0][D:D + 1, :], 1.0)
            nc.vector.memset(hidden[1][D:D + 1, :], 1.0).then_inc(ones_set, 1)

            x3 = x_all[:].rearrange("p (j d) -> p j d", d=D)
            h3 = h_all[:].rearrange("p (j d) -> p j d", d=D)
            dve.wait_ge(x_in, 16 * len(spread))
            for j in range(PER):
                last = nc.vector.bn_stats(stats[:, j, :], x3[:, j, :])
            ordered(last)
            for j in range(PER):
                last = nc.vector.bn_aggr(moments[:, j, :], stats[:, j, :])
            last.then_inc(stats_done, 1)
            dve.wait_ge(stats_done, 1)
            ordered(nc.vector.tensor_tensor(h3, x3, moments[:, :, 0:1].broadcast_to((NP, PER, D)), ALU.subtract))
            dve.wait_ge(std_done, 1)
            ordered(nc.vector.reciprocal(rstd[:], std[:]))
            nc.vector.tensor_tensor(h3, h3, rstd[:].unsqueeze(2).broadcast_to((NP, PER, D)), ALU.mult).then_inc(normed, 1)

            dve.wait_ge(dst_in, 16)
            nc.vector.tensor_reduce(first_last[:, 0:1], dst_by_row[:], AX.X, ALU.min).then_inc(bounds_min_max, 1)
            nc.vector.tensor_reduce(first_last[:, 1:2], dst_by_row[:], AX.X, ALU.max).then_inc(bounds_min_max, 1)
            dve.wait_ge(weights_in, 16 * N_WEIGHTS)
            nc.vector.tensor_scalar(scale_one_eps[:], scale_eps[:], 1.0, None, ALU.add).then_inc(one_eps_set, 1)
            dve.wait_ge(bounds_spread, 1)
            nc.vector.tensor_copy(bounds_f[:], agg_ps[:, 0:2 * ROWS]).then_inc(bounds_ready, 1)
            nc.vector.tensor_copy(bounds_i[:], agg_ps[0:1, 0:2 * ROWS]).then_inc(bounds_ready, 1)
            dve.wait_ge(bounds_ready, 2)
            dve.wait_ge(iota_copied, 1)
            dve.wait_ge(acc_ready, NCH)

            window = dve.alloc_register("dve_window")
            dve.reg_mov(window, 1)
            offsets = dve.alloc_register("dve_offsets")
            dve.reg_mov(offsets, 1)

            def sum_windows(row, tiles, parts):
                first = dve.value_load(bounds_i[0:1, bass.ds(row, 1)], min_val=0, max_val=N - 1)
                last = dve.value_load(bounds_i[0:1, bass.ds(row + ROWS, 1)], min_val=0, max_val=N - 1)
                with dve.Fori(first, last + 1, WINDOW) as base:
                    this_window, this_offset = dve.snap(window), dve.snap(offsets)
                    dve.wait_ge(offsets_made, this_offset)
                    nc.vector.tensor_tensor(
                        select[0:parts, 0:tiles, :],
                        iota_ps[0:parts, 0:WINDOW].unsqueeze(1).broadcast_to((parts, tiles, WINDOW)),
                        dst_rel[0:parts, 0:tiles].unsqueeze(2).broadcast_to((parts, tiles, WINDOW)),
                        ALU.is_equal).then_inc(select_made, 1)
                    dve.wait_ge(agg_done, this_window)
                    dve.wait_ge(acc_summed, this_window)
                    nc.vector.tensor_tensor(acc[:, bass.ds(base, WINDOW)], acc[:, bass.ds(base, WINDOW)],
                                            agg_ps[0:D, 0:WINDOW], ALU.add).then_inc(acc_summed, 1)
                    nc.vector.tensor_scalar(dst_rel[0:parts, 0:tiles], dst_rel[0:parts, 0:tiles], float(-WINDOW), None,
                                            ALU.add).then_inc(offsets_made, 1)
                    dve.reg_add(offsets, offsets, 1)
                    dve.reg_add(window, window, 1)

            def relative(source, row, parts, tiles, arrived, count):
                last_offset = dve.snap(offsets)
                dve.wait_ge(arrived, count)
                dve.wait_ge(offsets_made, last_offset)
                nc.vector.tensor_scalar(dst_rel[0:parts, 0:tiles], source, bounds_f[0:parts, bass.ds(row, 1)], None,
                                        ALU.subtract).then_inc(offsets_made, 1)
                dve.reg_add(offsets, offsets, 1)

            def add_half(b, i, gathered_by, edge_count):
                dve.wait_ge(edge_done, edge_count)
                dve.wait_ge(gather_in[b][i], gathered_by)
                nc.vector.tensor_tensor(msg[b][:, i * HALF:(i + 1) * HALF], edge_ps[b][i][:, 0:HALF],
                                        gathered[b][:, i * HALF:(i + 1) * HALF], ALU.add).then_inc(added, 1)

            def group(b, row, meta_by, gathered_by, edge_count):
                relative(meta[b][:, GROUP_TILES:2 * GROUP_TILES], row, 128, GROUP_TILES, meta_in[b], meta_by)
                for i in range(2):
                    add_half(b, i, gathered_by, edge_count)
                sum_windows(row, GROUP_TILES, 128)

            with dve.Fori(0, PAIRS) as p:
                for b in range(2):
                    group(b, 2 * p + b, 16 * p + 16, 16 * HALF_TILES * (p + 1), 2 * p + b + 1)
            group(0, GROUPS - 1, 16 * PAIRS + 16, 16 * HALF_TILES * (PAIRS + 1), GROUPS)
            relative(dst_tail_in[:, 0:1], GROUPS, TAIL, 1, tail_in, 48)
            dve.wait_ge(edge_done, GROUPS + 1)
            dve.wait_ge(tail_gather_in, 16)
            nc.vector.tensor_tensor(msg[1][0:TAIL, 0:D], edge_ps[1][0][0:TAIL, 0:D], gathered[1][0:TAIL, 0:D],
                                    ALU.add).then_inc(added, 1)
            sum_windows(GROUPS, 1, TAIL)
            nc.vector.memset(eps_col[:], 0.0).then_inc(acc_final, 1)

            for c, (j0, j1) in enumerate(node_chunks):
                dve.wait_ge(mlp2_done, c + 1)
                nc.vector.tensor_tensor(x_all[:, j0 * D:j1 * D], x_all[:, j0 * D:j1 * D],
                                        edge_ps[0][c % 2][0:NP, 0:(j1 - j0) * D], ALU.add).then_inc(result_done, 1)


def kernel(x, src, dst, edge_attr_96, L0_gnn_W_edge, L0_gnn_b_edge, L0_gnn_eps, L0_gnn_W1, L0_gnn_b1, L0_gnn_W2,
           L0_gnn_b2):
    import concourse.bacc as bacc
    from concourse.bass_utils import run_bass_kernel_spmd

    x, src, dst, edge = (np.asarray(a) for a in (x, src, dst, edge_attr_96))
    E, D = edge.shape
    GE = GROUP_TILES * EDGE_TILE
    groups = E // GE
    body = groups * GE

    def by_tile(index):
        return index[:body].reshape(groups, GROUP_TILES, EDGE_TILE).transpose(0, 2, 1)

    laid_out = {
        "x": x,
        "edge_blocks": edge[:body].reshape(groups, GE, D).transpose(0, 2, 1),
        "edge_tail": edge[body:].T,
        "meta_blocks": np.concatenate([by_tile(src), by_tile(dst)], axis=2),
        "src_tail": src[body:],
        "dst_tail": dst[body:],
        "dst_rows": np.pad(dst, (0, body + GE - E), mode="edge").reshape(groups + 1, GE),
        "w_edge_t": np.asarray(L0_gnn_W_edge).T,
        "b_edge": np.asarray(L0_gnn_b_edge),
        "eps": np.asarray(L0_gnn_eps).reshape(1),
        "w1_t": np.asarray(L0_gnn_W1).T,
        "b1": np.asarray(L0_gnn_b1),
        "w2_t": np.asarray(L0_gnn_W2).T,
        "b2": np.asarray(L0_gnn_b2),
    }
    nc = bacc.Bacc("TRN2", target_bir_lowering=False, num_devices=1)
    arrays, args = {}, {}
    for name, a in laid_out.items():
        a = np.ascontiguousarray(a)
        arrays[f"{name}_dram"] = a
        args[name] = nc.dram_tensor(f"{name}_dram", a.shape, mybir.dt.from_np(a.dtype), kind="ExternalInput").ap()
    out = nc.dram_tensor("out_dram", x.shape, F32, kind="ExternalOutput").ap()
    gnn_layer(nc, out=out, **args)
    result = run_bass_kernel_spmd(nc, [arrays], core_ids=[0])
    return result.results[0]["out_dram"]
```
